# Optimizing a Trainium2 kernel written in Bass

```python
import numpy as np
import jax
import jax.numpy as jnp

def _softmax(x, axis=-1):
    return jax.nn.softmax(x, axis=axis)

def _gelu(x):
    return jax.nn.gelu(x, approximate=True)

def _silu(x):
    return jax.nn.silu(x)

def _sigmoid(x):
    return jax.nn.sigmoid(x)

def _layernorm(x, axis=-1, eps=1e-05):
    m = jnp.mean(x, axis=axis, keepdims=True)
    v = jnp.var(x, axis=axis, keepdims=True)
    return (x - m) / jnp.sqrt(v + eps)

def _scatter_add(tgt, idx, src, axis=0):
    return tgt.at[idx].add(src)

def _segment_sum(src, seg, n):
    return jax.ops.segment_sum(src, seg, n)
kernel_name = 'mk_adj_preln_d1_adj_r2_21d00f'

def setup_inputs(seed: int=0):
    np.random.seed(seed)
    _w = jnp.asarray

    def _rec_inputs():
        import jax
        import jax.numpy as jnp
        _gk = jax.random.key(seed)
        x = -0.0002928 + 1 * jax.random.normal(jax.random.fold_in(_gk, 1), (4096, 256), jnp.float32)
        _a = jax.random.bernoulli(jax.random.fold_in(_gk, 2), 0.000488281, (4096, 4096))
        _a = jnp.logical_or(_a, jnp.swapaxes(_a, -1, -2))
        _a = jnp.logical_or(_a, jnp.eye(4096, dtype=bool))
        _af = _a.astype(jnp.float32)
        _af = _af * jax.random.uniform(jax.random.fold_in(_gk, 3), (4096, 4096), jnp.float32, 0.05, 1)
        adj = _af
        return (x, adj)
    x, adj = _rec_inputs()

    def _L0_gnn_setup():
        import jax, jax.numpy as jnp
        import numpy as np
        N_NODES = 4096
        DIM = 256
        key = jax.random.key(seed)
        k1, k2, k3, k4 = jax.random.split(key, 4)
        x = jax.random.normal(k1, (N_NODES, DIM), dtype=jnp.float32)
        adj = jax.random.uniform(k2, (N_NODES, N_NODES), dtype=jnp.float32)
        bound = 1.0 / np.sqrt(DIM)
        W = jax.random.uniform(k3, (DIM, DIM), minval=-bound, maxval=bound, dtype=jnp.float32)
        b = jax.random.uniform(k4, (DIM,), minval=-bound, maxval=bound, dtype=jnp.float32)
        return {'x': x, 'adj': adj, 'W': W, 'b': b}
    _L0_gnn_all = _L0_gnn_setup()
    _L0_gnn_in = {k: v for k, v in _L0_gnn_all.items() if k in ('W', 'b')}
    del _L0_gnn_all
    return {'x': x, 'adj': adj, 'L0_gnn_W': _L0_gnn_in['W'], 'L0_gnn_b': _L0_gnn_in['b']}

def reference(x, adj, L0_gnn_W, L0_gnn_b):
    import jax
    import jax.numpy as jnp

    def _L0_gnn_ref(x, adj, W, b):
        import jax, jax.numpy as jnp
        import numpy as np
        N_NODES = 4096
        DIM = 256
        agg = jnp.matmul(adj, x)
        out = jnp.matmul(agg, W.T) + b
        return jax.nn.relu(out)
    h = jnp.maximum(_layernorm(x, axis=-1), 0.0)
    x = x + _L0_gnn_ref(h, adj, L0_gnn_W, L0_gnn_b)
    return x

_drawn_inputs = setup_inputs


def setup_inputs(seed=0):
    import zlib

    import numpy as np

    out = dict(_drawn_inputs(seed))
    spreads = {}
    factors = {'L0_gnn_b': 2.722}
    for name, (base, spread) in spreads.items():
        noise = np.random.default_rng([zlib.crc32(name.encode()), seed]).standard_normal(out[name].shape)
        drawn = base * np.exp(spread * noise) if base else spread * noise
        out[name] = jnp.asarray(drawn.astype(out[name].dtype))
    for name, factor in factors.items():
        out[name] = (out[name] * factor).astype(out[name].dtype)
    return out
```

```python
import concourse.bass as bass
from concourse import mybir
from contextlib import ExitStack

P = 128


def bass_preln_gnn_residual(
    nc: bass.Bass,
    x: bass.AP,
    x_t: bass.AP,
    adj_t: bass.AP,
    w_t: bass.AP,
    b_cols: bass.AP,
    out_t: bass.AP,
):
    fp32 = mybir.dt.float32
    fp32r = mybir.dt.float32r
    ALU = mybir.AluOpType
    ACT = mybir.ActivationFunctionType

    N, D = x.shape
    TILES = N // P
    KB = D // P
    BANK = 512
    CHUNKS = 2
    GW = CHUNKS * BANK
    GROUPS = N // GW
    SUMS = KB * CHUNKS
    U = 4
    QUADS = TILES // U
    EPS = 1e-5
    AHEAD = 2

    x_v = x.rearrange("(p t) d -> p t d", t=TILES)
    adj_v = adj_t.rearrange("(p t) i -> p t i", t=TILES)
    xt_v = x_t.rearrange("(o p) i -> p o i", p=P)
    out_v = out_t.rearrange("(o p) i -> p o i", p=P)
    wt_v = w_t.rearrange("(k p) o -> p k o", p=P)
    X_PIECES = [(0, 2), (2, U + 2), (U + 2, TILES)]

    ctx = ExitStack()
    with ctx:
        def sb(name, shape, dt=fp32):
            return ctx.enter_context(nc.sbuf_tensor(name, shape, dt))

        def sem(name):
            return ctx.enter_context(nc.semaphore(name))

        x_sb = sb("x_sb", [P, TILES, D])
        w_sb = sb("w_sb", [P, KB, D])
        b_sb = sb("b_sb", [P, KB])
        ident = sb("ident", [P, P])
        minus_half = sb("minus_half", [P, 1])
        stats = sb("stats", [P, U, 6])
        mean = sb("mean", [P, U])
        spread = sb("spread", [P, U])
        square = sb("square", [P, U])
        var_d = sb("var_d", [P, U])
        rstd = sb("rstd", [P, U])
        centred = sb("centred", [P, U, D])
        centred_t = sb("centred_t", [P, U, KB, P])
        z_store = sb("z_store", [P, TILES, 2, D], fp32r)
        z_ring = sb("z_ring", [P, U, 2, D], fp32r)
        adj_in = sb("adj_in", [P, U, GW])
        adj_hi = sb("adj_hi", [P, U, GW], fp32r)
        adj_lo = sb("adj_lo", [P, U, GW], fp32r)
        xt_sb = sb("xt_sb", [P, KB, GW])
        out_sb = sb("out_sb", [P, KB, GW])

        banks = [ctx.enter_context(nc.psum_tensor(f"bank{i}", [P, BANK], fp32)) for i in range(2 * SUMS)]
        turned = banks[SUMS:SUMS + 2]
        z_psum = banks[SUMS + 2:SUMS + 4]

        s_w = sem("w_landed")
        s_b = sem("b_landed")
        s_x = [sem(f"x_landed{i}") for i in range(len(X_PIECES))]
        s_adj = [sem(f"adj_landed{i}") for i in range(U)]
        s_xt = sem("xt_landed")
        s_ident0 = sem("ident_cleared")
        s_ident = sem("ident_ready")
        s_half = sem("minus_half_ready")
        s_stats = sem("stats_made")
        s_mean = sem("mean_made")
        s_spread = sem("spread_made")
        s_square = sem("square_made")
        s_var = sem("var_d_made")
        s_w16 = sem("w_scaled")
        s_centred = sem("centred_made")
        s_rstd = sem("rstd_made")
        s_turn = sem("transposed")
        s_ct = sem("centred_t_made")
        s_zmm = sem("z_product_done")
        s_zhi = sem("z_hi_made")
        s_zlo = sem("z_lo_made")
        s_zst = sem("z_stored")
        s_zring = sem("z_staged")
        s_hi = sem("adj_hi_made")
        s_lo = sem("adj_lo_made")
        s_pe = sem("tiles_summed")
        s_relu = sem("relu_made")
        s_sum = sem("residual_added")
        s_out = sem("out_stored")
        s_last = [sem(f"out_stored_last{i}") for i in range(SUMS)]

        block = ctx.enter_context(nc.Block())

        def sum_bank(g, o, c):
            return banks[(g % 2) * SUMS + o * CHUNKS + c]

        def over_quads(eng, body, first, last):
            lo, hi = (1 if first else 0), (QUADS - 1 if last else QUADS)
            if first:
                body(0, True, False)
            with eng.Fori(lo, hi) as q:
                body(q, False, False)
            if last:
                body(QUADS - 1, False, True)

        @block.sync
        def _(sp):
            def load_x(i):
                a, b = X_PIECES[i]
                sp.dma_start(x_sb[:, a:b, :], x_v[:, a:b, :]).then_inc(s_x[i], 16)

            def load_adj(g, q, k, first):
                if not first:
                    sp.wait_ge(s_hi, g * TILES + (q - 1) * U + k + 1)
                    sp.wait_ge(s_lo, g * TILES + (q - 1) * U + k + 1)
                sp.dma_start(adj_in[:, k, :], adj_v[:, bass.ds(q * U + k, 1), g * GW:(g + 1) * GW]
                             ).then_inc(s_adj[k], 16)

            load_x(0)
            sp.dma_start(w_sb[:], wt_v).then_inc(s_w, 16)
            load_adj(0, 0, 0, True)
            load_x(1)
            for k in range(1, U):
                load_adj(0, 0, k, True)
            load_x(2)
            for g in range(GROUPS):
                with sp.Fori(1 if g == 0 else 0, QUADS) as q:
                    for k in range(U):
                        load_adj(g, q, k, False)
            for o in range(KB):
                for c in range(CHUNKS):
                    i = o * CHUNKS + c
                    sp.wait_ge(s_sum, (GROUPS - 1) * SUMS + i + 1)
                    at = (GROUPS - 1) * GW + c * BANK
                    sp.dma_start(out_v[:, o, at:at + BANK], out_sb[:, o, c * BANK:(c + 1) * BANK]
                                 ).then_inc(s_last[i], 16)
            for s in s_last:
                sp.wait_ge(s, 16)
            sp.wait_ge(s_out, 16 * (GROUPS - 1))

        @block.gpsimd
        def _(pool):
            nc.gpsimd.memset(ident[:], 0.0).then_inc(s_ident0, 1)
            nc.gpsimd.memset(minus_half[:], -0.5).then_inc(s_half, 1)
            pool.wait_ge(s_ident0, 1)
            nc.gpsimd.affine_select(out=ident[:], in_=ident[:], compare_op=ALU.not_equal, fill=1.0,
                                    base=0, pattern=[[-1, P]], channel_multiplier=1).then_inc(s_ident, 1)
            pool.dma_start(b_sb[:], b_cols).then_inc(s_b, 16)
            pool.wait_ge(s_half, 1)

            def root(t, k, fresh):
                pool.wait_ge(s_var, t + 1)
                if not fresh:
                    pool.wait_ge(s_zlo, t - U + 1)
                nc.gpsimd.tensor_tensor(rstd[:, k:k + 1], var_d[:, k:k + 1], minus_half[:],
                                        ALU.pow).then_inc(s_rstd, 1)

            def keep_z(t, k):
                pool.wait_ge(s_zlo, t + 1)
                nc.gpsimd.tensor_copy(z_store[:, bass.ds(t, 1), :, :], z_ring[:, k, :, :].bitcast(fp32)
                                      ).then_inc(s_zst, 1)

            def quad0(q, first, last):
                for k in range(U):
                    t = q * U + k
                    if not (last and k + AHEAD >= U):
                        root(t + AHEAD, (k + AHEAD) % U, first and k + AHEAD < U)
                    keep_z(t, k)

            for t in range(AHEAD):
                root(t, t, True)
            over_quads(pool, quad0, True, True)
            pool.dma_start(xt_sb[:], xt_v[:, :, 0:GW]).then_inc(s_xt, 16)
            for g in range(GROUPS - 1):
                pool.wait_ge(s_sum, (g + 1) * SUMS)
                pool.dma_start(out_v[:, :, g * GW:(g + 1) * GW], out_sb[:]).then_inc(s_out, 16)
                pool.dma_start(xt_sb[:], xt_v[:, :, (g + 1) * GW:(g + 2) * GW]).then_inc(s_xt, 16)

        @block.vector
        def _(dve):
            def adj_rest(g, q, k):
                n = g * TILES + q * U + k
                dve.wait_ge(s_hi, n + 1)
                nc.vector.tensor_tensor(adj_lo[:, k, :], adj_in[:, k, :], adj_hi[:, k, :].bitcast(fp32),
                                        ALU.subtract).then_inc(s_lo, 1)

            def tile_stats(t, k):
                nc.vector.bn_stats(stats[:, k, :], x_sb[:, bass.ds(t, 1), :]).then_inc(s_stats, 1)

            def tile_centre(t, k, fresh):
                even, odd = stats[:, k, 0:3], stats[:, k, 3:6]
                dve.wait_ge(s_stats, t + 1)
                nc.vector.tensor_scalar(mean[:, k:k + 1], even[:, 1:2], odd[:, 1:2], 0.5,
                                        ALU.add, ALU.mult).then_inc(s_mean, 1)
                nc.vector.tensor_scalar(spread[:, k:k + 1], even[:, 1:2], odd[:, 1:2], D ** 0.5 / 2,
                                        ALU.subtract, ALU.mult).then_inc(s_spread, 1)
                dve.wait_ge(s_mean, t + 1)
                if not fresh:
                    dve.wait_ge(s_turn, t - U + 1)
                nc.vector.tensor_scalar(centred[:, k, :], x_sb[:, bass.ds(t, 1), :],
                                        mean[:, k:k + 1], 0.0, ALU.subtract, ALU.max
                                        ).then_inc(s_centred, 1)
                dve.wait_ge(s_spread, t + 1)
                nc.vector.scalar_tensor_tensor(out=square[:, k:k + 1], in0=spread[:, k:k + 1],
                                               scalar=spread[:, k:k + 1], in1=even[:, 2:3],
                                               op0=ALU.mult, op1=ALU.add).then_inc(s_square, 1)
                dve.wait_ge(s_square, t + 1)
                if not fresh:
                    dve.wait_ge(s_rstd, t - U + 1)
                nc.vector.tensor_scalar(var_d[:, k:k + 1], square[:, k:k + 1], odd[:, 2:3], D * EPS,
                                        ALU.add, ALU.add).then_inc(s_var, 1)

            def z_rest(t, k):
                dve.wait_ge(s_zhi, t + 1)
                nc.vector.scalar_tensor_tensor(out=z_ring[:, k, 1, :], in0=z_psum[k % 2][:, 0:D],
                                               scalar=rstd[:, k:k + 1],
                                               in1=z_ring[:, k, 0, :].bitcast(fp32),
                                               op0=ALU.mult, op1=ALU.subtract).then_inc(s_zlo, 1)

            def quad0(q, first, last):
                for k in range(U):
                    t = q * U + k
                    ka = (k + AHEAD) % U
                    ahead = not (last and k + AHEAD >= U)
                    fresh = first and k + AHEAD < U
                    if ahead:
                        tile_stats(t + AHEAD, ka)
                    adj_rest(0, q, k)
                    if ahead:
                        tile_centre(t + AHEAD, ka, fresh)
                    z_rest(t, k)

            dve.wait_ge(s_x[0], 16)
            for t in range(AHEAD):
                tile_stats(t, t)
                tile_centre(t, t, True)
            dve.wait_ge(s_w, 16)
            nc.vector.tensor_scalar(w_sb[:], w_sb[:], D ** 0.5, None, ALU.mult).then_inc(s_w16, 1)
            dve.wait_ge(s_x[1], 16)
            quad0(0, True, False)
            dve.wait_ge(s_x[2], 16)
            with dve.Fori(1, QUADS - 1) as q:
                quad0(q, False, False)
            quad0(QUADS - 1, False, True)

            def add_residual(g):
                dve.wait_ge(s_xt, 16 * (g + 1))
                for o in range(KB):
                    for c in range(CHUNKS):
                        dve.wait_ge(s_relu, g * SUMS + o * CHUNKS + c + 1)
                        cols = slice(c * BANK, (c + 1) * BANK)
                        nc.vector.tensor_tensor(out_sb[:, o, cols], out_sb[:, o, cols], xt_sb[:, o, cols],
                                                ALU.add).then_inc(s_sum, 1)

            for g in range(1, GROUPS):
                for k in range(U):
                    adj_rest(g, 0, k)
                add_residual(g - 1)
                with dve.Fori(1, QUADS) as q:
                    for k in range(U):
                        adj_rest(g, q, k)
            add_residual(GROUPS - 1)

        @block.scalar
        def _(act):
            def adj_rounded(g, q, k, fresh):
                n = g * TILES + q * U + k
                act.wait_ge(s_adj[k], 16 * (g * QUADS + q + 1))
                if not fresh:
                    act.wait_ge(s_pe, n - U + 1)
                nc.scalar.activation(adj_hi[:, k, :], adj_in[:, k, :], ACT.Copy).then_inc(s_hi, 1)

            def stage_z(g, q, k):
                nc.scalar.activation(z_ring[:, k, :, :], z_store[:, bass.ds(q * U + k, 1), :, :].bitcast(fp32),
                                     ACT.Copy).then_inc(s_zring, 1)

            def take_turned(t, k, fresh):
                act.wait_ge(s_turn, t + 1)
                if not fresh:
                    act.wait_ge(s_zmm, t - U + 1)
                nc.scalar.activation(centred_t[:, k, :, :],
                                     turned[k % 2][:, 0:D].rearrange("p (b j) -> p b j", b=KB),
                                     ACT.Copy).then_inc(s_ct, 1)

            def z_rounded(t, k, fresh):
                if not fresh:
                    act.wait_ge(s_pe, t - U + 1)
                    act.wait_ge(s_zst, t - U + 1)
                act.wait_ge(s_zmm, t + 1)
                act.wait_ge(s_rstd, t + 1)
                nc.scalar.activation(z_ring[:, k, 0, :], z_psum[k % 2][:, 0:D],
                                     ACT.Copy, scale=rstd[:, k:k + 1]).then_inc(s_zhi, 1)

            def quad0(q, first, last):
                for k in range(U):
                    t = q * U + k
                    adj_rounded(0, q, k, first)
                    if not (last and k == U - 1):
                        take_turned(t + 1, (k + 1) % U, first and k < U - 1)
                    z_rounded(t, k, first)

            take_turned(0, 0, True)
            over_quads(act, quad0, True, True)

            def relu_out(g):
                act.wait_ge(s_pe, (g + 1) * TILES)
                if g >= 1:
                    act.wait_ge(s_out, 16 * g)
                for o in range(KB):
                    for c in range(CHUNKS):
                        nc.scalar.activation(out_sb[:, o, c * BANK:(c + 1) * BANK], sum_bank(g, o, c)[:],
                                             ACT.Relu, bias=b_sb[:, o:o + 1]).then_inc(s_relu, 1)

            act.wait_ge(s_b, 16)
            act.wait_ge(s_zst, TILES)
            for g in range(1, GROUPS):
                for k in range(U):
                    adj_rounded(g, 0, k, False)
                    stage_z(g, 0, k)
                relu_out(g - 1)
                with act.Fori(1, QUADS) as q:
                    for k in range(U):
                        adj_rounded(g, q, k, False)
                        stage_z(g, q, k)
            relu_out(GROUPS - 1)

        @block.tensor
        def _(pe):
            def turn(t, k, fresh):
                pe.wait_ge(s_centred, t + 1)
                if not fresh:
                    pe.wait_ge(s_ct, t - 1)
                for b in range(KB):
                    last = nc.tensor.transpose(turned[k % 2][:, b * P:(b + 1) * P],
                                               centred[:, k, b * P:(b + 1) * P], ident[:])
                last.then_inc(s_turn, 1)

            def z_product(t, k, fresh):
                pe.wait_ge(s_ct, t + 1)
                if not fresh:
                    pe.wait_ge(s_zlo, t - 1)
                for b in range(KB):
                    last = nc.tensor.matmul(z_psum[k % 2][:, 0:D], centred_t[:, k, b, :], w_sb[:, b, :],
                                            start=(b == 0), stop=(b == KB - 1))
                last.then_inc(s_zmm, 1)

            def sum_tile(g, q, k, start):
                n = g * TILES + q * U + k
                if g == 0:
                    pe.wait_ge(s_zlo, n + 1)
                else:
                    pe.wait_ge(s_zring, n - TILES + 1)
                pe.wait_ge(s_lo, n + 1)
                for o in range(KB):
                    cols = slice(o * P, (o + 1) * P)
                    for z_part, adj_part in ((0, adj_hi), (0, adj_lo), (1, adj_hi)):
                        for c in range(CHUNKS):
                            begins = start and z_part == 0 and adj_part is adj_hi
                            last = nc.tensor.matmul(sum_bank(g, o, c)[:], z_ring[:, k, z_part, cols],
                                                    adj_part[:, k, c * BANK:(c + 1) * BANK],
                                                    start=begins, stop=(z_part == 1), skip_group_check=True)
                last.then_inc(s_pe, 1)

            def quad0(q, first, last):
                for k in range(U):
                    t = q * U + k
                    sum_tile(0, q, k, first and k == 0)
                    if not (last and k + 3 >= U):
                        turn(t + 3, (k + 3) % U, False)
                    if not (last and k + 2 >= U):
                        z_product(t + 2, (k + 2) % U, False)

            pe.wait_ge(s_ident, 1)
            pe.wait_ge(s_w16, 1)
            turn(0, 0, True)
            turn(1, 1, True)
            z_product(0, 0, True)
            turn(2, 2, False)
            z_product(1, 1, True)
            over_quads(pe, quad0, True, True)
            for g in range(1, GROUPS):
                if g >= 2:
                    pe.wait_ge(s_relu, (g - 1) * SUMS)
                for k in range(U):
                    sum_tile(g, 0, k, k == 0)
                with pe.Fori(1, QUADS) as q:
                    for k in range(U):
                        sum_tile(g, q, k, False)


def kernel(x, adj, L0_gnn_W, L0_gnn_b):
    import numpy as np
    import concourse.bacc as bacc
    from concourse.bass_utils import run_bass_kernel_spmd

    x, adj, w, b = (np.asarray(a) for a in (x, adj, L0_gnn_W, L0_gnn_b))
    nodes, features = x.shape
    arrays = {
        "x_dram": np.ascontiguousarray(x),
        "x_t_dram": np.ascontiguousarray(x.T),
        "adj_t_dram": np.ascontiguousarray(adj.T),
        "w_t_dram": np.ascontiguousarray(w.T),
        "b_cols_dram": np.ascontiguousarray(b.reshape(features // P, P).T),
    }
    nc = bacc.Bacc("TRN2", target_bir_lowering=False, num_devices=1)
    args = [nc.dram_tensor(name, a.shape, mybir.dt.from_np(a.dtype), kind="ExternalInput").ap()
            for name, a in arrays.items()]
    out_t = nc.dram_tensor("out_t_dram", (features, nodes), mybir.dt.float32, kind="ExternalOutput").ap()
    bass_preln_gnn_residual(nc, *args, out_t)
    r = run_bass_kernel_spmd(nc, [arrays], core_ids=[0])
    return np.ascontiguousarray(r.results[0]["out_t_dram"].T)
```

```python
import concourse.bass as bass
from concourse import mybir
from contextlib import ExitStack

P = 128


def bass_preln_gnn_residual(
    nc: bass.Bass,
    x: bass.AP,
    x_t: bass.AP,
    adj_t: bass.AP,
    w_t: bass.AP,
    b_cols: bass.AP,
    out_t: bass.AP,
):
    fp32 = mybir.dt.float32
    fp32r = mybir.dt.float32r
    ALU = mybir.AluOpType
    ACT = mybir.ActivationFunctionType

    N, D = x.shape
    TILES = N // P
    KB = D // P
    BANK = 512
    CHUNKS = 2
    GW = CHUNKS * BANK
    GROUPS = N // GW
    LAST = GROUPS - 1
    SUMS = KB * CHUNKS
    U = 4
    QUADS = TILES // U
    AHEAD = 2
    EPS = 1e-5
    WARM_UP = 11

    x_v = x.rearrange("(p t) d -> p t d", t=TILES)
    adj_v = adj_t.rearrange("(p t) i -> p t i", t=TILES)
    xt_v = x_t.rearrange("(o p) i -> p o i", p=P)
    out_v = out_t.rearrange("(o p) i -> p o i", p=P)
    wt_v = w_t.rearrange("(k p) o -> p k o", p=P)

    ctx = ExitStack()
    with ctx:
        def sb(name, shape, dt=fp32):
            return ctx.enter_context(nc.sbuf_tensor(name, shape, dt))

        def sem(name):
            return ctx.enter_context(nc.semaphore(name))

        x_sb = sb("x_sb", [P, TILES, D])
        w_sb = sb("w_sb", [P, KB, D])
        w_hi = sb("w_hi", [P, KB, D], fp32r)
        w_lo = sb("w_lo", [P, KB, D], fp32r)
        b_sb = sb("b_sb", [P, KB])
        minus_half = sb("minus_half", [P, 1])
        eps_d = sb("eps_d", [P, 1])
        total = sb("total", [P, U])
        neg_mean = sb("neg_mean", [P, U])
        squares = sb("squares", [P, U, D])
        square_sum = sb("square_sum", [P, U])
        var_d = sb("var_d", [P, U])
        rstd = sb("rstd", [P, U])
        warm = sb("warm", [P, BANK], mybir.dt.bfloat16)
        centred = sb("centred", [P, U, D])
        h_ring = sb("h_ring", [P, U, 2, D], fp32r)
        h_store = sb("h_store", [P, TILES, 2, D])
        adj_in = sb("adj_in", [P, U, GW])
        adj_hi = sb("adj_hi", [P, U, GW], fp32r)
        adj_lo = sb("adj_lo", [P, U, GW], fp32r)
        agg_hi = sb("agg_hi", [P, KB, GW], fp32r)
        agg_lo = sb("agg_lo", [P, KB, GW], fp32r)
        xt_sb = sb("xt_sb", [P, KB, GW])
        out_sb = sb("out_sb", [P, KB, GW])

        banks = [ctx.enter_context(nc.psum_tensor(f"bank{i}", [P, BANK], fp32)) for i in range(2 * SUMS)]

        s_w = sem("w_landed")
        s_b = sem("b_landed")
        s_x0 = [sem(f"first_x_landed{t}") for t in range(AHEAD)]
        s_x = sem("x_landed")
        s_adj = [sem(f"adj_landed{i}") for i in range(U)]
        s_adj0 = [sem(f"first_adj_landed{c}") for c in range(CHUNKS)]
        s_xt = sem("xt_landed")
        s_const = sem("constants_ready")
        s_warm = sem("warm_ready")
        s_whi = sem("w_hi_made")
        s_wlo = sem("w_lo_made")
        s_total = sem("total_made")
        s_mean = sem("neg_mean_made")
        s_square = sem("square_sum_made")
        s_var = sem("var_d_made")
        s_rstd = sem("rstd_made")
        s_centred = sem("centred_made")
        s_hhi = sem("h_hi_made")
        s_hlo = sem("h_lo_made")
        s_hst = [sem(f"h_stored{k}") for k in range(U)]
        s_hring = sem("h_staged")
        s_hi = sem("adj_hi_made")
        s_hi0 = sem("first_adj_hi_chunks_made")
        s_lo = sem("adj_lo_made")
        s_pe = sem("tiles_summed")
        s_chunk = sem("last_group_chunk_summed")
        s_ahi = sem("agg_hi_made")
        s_alo = sem("agg_lo_made")
        s_prod = sem("w_products_done")
        s_relu = sem("relu_made")
        s_sum = sem("residual_added")
        s_out = sem("out_stored")
        s_last = [sem(f"out_stored_last{i}") for i in range(SUMS + 1)]

        block = ctx.enter_context(nc.Block())

        def bank(g, block_, c):
            return banks[(g % 2) * SUMS + c * KB + block_]

        GROUP_BANKS = [(c, kb) for c in range(CHUNKS) for kb in range(KB)]

        def chunk(c):
            return slice(c * BANK, (c + 1) * BANK)

        def pieces(g):
            whole = [(c, o, 0, BANK) for c, o in GROUP_BANKS]
            if g < LAST:
                return whole
            c, o, _, _ = whole.pop()
            return whole + [(c, o, 0, BANK // 2), (c, o, BANK // 2, BANK)]

        def within(c, a, b):
            return slice(c * BANK + a, c * BANK + b)

        def product(g, c, o, a, b):
            return bank(g if a == 0 else g + 1, o, c)[:, a:b]

        @block.sync
        def _(sp):
            def load_x(q, tiles):
                at = bass.ds(q * U + AHEAD, tiles)
                sp.dma_start(x_sb[:, at, :], x_v[:, at, :]).then_inc(s_x, 16)

            def load_adj(g, q, k, fresh):
                if not fresh:
                    sp.wait_ge(s_hi, g * TILES + (q - 1) * U + k + 1)
                    sp.wait_ge(s_lo, g * TILES + (q - 1) * U + k + 1)
                sp.dma_start(adj_in[:, k, :], adj_v[:, bass.ds(q * U + k, 1), g * GW:(g + 1) * GW]
                             ).then_inc(s_adj[k], 16)

            def keep_h(q, k):
                sp.wait_ge(s_hlo, q * U + k + 1)
                sp.dma_start(h_store[:, bass.ds(q * U + k, 1), :, :], h_ring[:, k, :, :].bitcast(fp32)).then_inc(s_hst[k], 16)

            def quad0(q, x_tiles):
                sp.wait_ge(s_x, 16 * q)
                load_x(q, x_tiles)
                for k in range(U):
                    load_adj(0, q, k, False)
                    keep_h(q - 1, k)

            for i in range(max(AHEAD, CHUNKS)):
                if i < AHEAD:
                    sp.dma_start(x_sb[:, i, :], x_v[:, i, :]).then_inc(s_x0[i], 16)
                if i < CHUNKS:
                    sp.dma_start(adj_in[:, 0, chunk(i)], adj_v[:, 0, chunk(i)]).then_inc(s_adj0[i], 16)
            load_adj(0, 0, 1, True)
            load_x(0, U)
            for k in range(2, U):
                load_adj(0, 0, k, True)
            with sp.Fori(1, QUADS - 1) as q:
                quad0(q, U)
            quad0(QUADS - 1, U - AHEAD)
            for k in range(U):
                load_adj(1, 0, k, False)
                keep_h(QUADS - 1, k)
            for g in range(1, GROUPS):
                with sp.Fori(1 if g == 1 else 0, QUADS) as q:
                    for k in range(U):
                        load_adj(g, q, k, False)
            for i, (c, o, a, b) in enumerate(pieces(LAST)):
                sp.wait_ge(s_sum, LAST * SUMS + i + 1)
                at = LAST * GW + c * BANK
                sp.dma_start(out_v[:, o, at + a:at + b], out_sb[:, o, within(c, a, b)]).then_inc(s_last[i], 16)
            for s in s_last:
                sp.wait_ge(s, 16)
            sp.wait_ge(s_out, 16 * LAST)

        @block.gpsimd
        def _(pool):
            nc.gpsimd.memset(minus_half[:], -0.5).then_inc(s_const, 1)
            nc.gpsimd.memset(eps_d[:], D * EPS).then_inc(s_const, 1)
            pool.wait_ge(s_const, 2)

            def root(t, k, fresh):
                pool.wait_ge(s_square, t + 1)
                nc.gpsimd.tensor_tensor(var_d[:, k:k + 1], square_sum[:, k:k + 1], eps_d[:],
                                        ALU.add).then_inc(s_var, 1)
                pool.wait_ge(s_var, t + 1)
                if not fresh:
                    pool.wait_ge(s_hlo, t - U + 1)
                nc.gpsimd.tensor_tensor(rstd[:, k:k + 1], var_d[:, k:k + 1], minus_half[:],
                                        ALU.pow).then_inc(s_rstd, 1)

            for t in range(AHEAD):
                root(t, t, True)
            for k in range(U):
                root(k + AHEAD, (k + AHEAD) % U, k + AHEAD < U)
            pool.dma_start(w_sb[:], wt_v).then_inc(s_w, 16)
            pool.dma_start(b_sb[:], b_cols).then_inc(s_b, 16)
            with pool.Fori(1, QUADS - 1) as q:
                for k in range(U):
                    root(q * U + k + AHEAD, (k + AHEAD) % U, False)
            for t in range(TILES - U + AHEAD, TILES):
                root(t, t % U, False)
            pool.dma_start(xt_sb[:], xt_v[:, :, 0:GW]).then_inc(s_xt, 16)
            for g in range(LAST):
                pool.wait_ge(s_sum, (g + 1) * SUMS)
                pool.dma_start(out_v[:, :, g * GW:(g + 1) * GW], out_sb[:]).then_inc(s_out, 16)
                pool.dma_start(xt_sb[:], xt_v[:, :, (g + 1) * GW:(g + 2) * GW]).then_inc(s_xt, 16)

        @block.vector
        def _(dve):
            def adj_rest(g, q, k):
                dve.wait_ge(s_hi, g * TILES + q * U + k + 1)
                nc.vector.tensor_tensor(adj_lo[:, k, :], adj_in[:, k, :], adj_hi[:, k, :].bitcast(fp32),
                                        ALU.subtract).then_inc(s_lo, 1)

            def first_adj_rest():
                for c in range(CHUNKS):
                    if c < CHUNKS - 1:
                        dve.wait_ge(s_hi0, c + 1)
                    else:
                        dve.wait_ge(s_hi, 1)
                    done = nc.vector.tensor_tensor(adj_lo[:, 0, chunk(c)], adj_in[:, 0, chunk(c)],
                                                   adj_hi[:, 0, chunk(c)].bitcast(fp32), ALU.subtract)
                done.then_inc(s_lo, 1)

            def add_up(t, k):
                nc.vector.reduce_sum(total[:, k:k + 1], x_sb[:, bass.ds(t, 1), :],
                                     mybir.AxisListType.XY).then_inc(s_total, 1)

            def centre(t, k, fresh):
                dve.wait_ge(s_total, t + 1)
                if not fresh:
                    dve.wait_ge(s_square, t - U + 1)
                nc.vector.tensor_scalar(neg_mean[:, k:k + 1], total[:, k:k + 1], -1.0 / D, None,
                                        ALU.mult).then_inc(s_mean, 1)
                dve.wait_ge(s_mean, t + 1)
                nc.vector.tensor_scalar(centred[:, k, :], x_sb[:, bass.ds(t, 1), :],
                                        neg_mean[:, k:k + 1], 0.0, ALU.add, ALU.max
                                        ).then_inc(s_centred, 1)

            def h_rest(t, k):
                dve.wait_ge(s_hhi, t + 1)
                nc.vector.scalar_tensor_tensor(out=h_ring[:, k, 1, :], in0=centred[:, k, :],
                                               scalar=rstd[:, k:k + 1],
                                               in1=h_ring[:, k, 0, :].bitcast(fp32),
                                               op0=ALU.mult, op1=ALU.subtract).then_inc(s_hlo, 1)

            def quad0(q, first, last):
                for k in range(U):
                    t = q * U + k
                    ka = (k + AHEAD) % U
                    ahead = not (last and k + AHEAD >= U)
                    if first and k == 0:
                        first_adj_rest()
                    else:
                        adj_rest(0, q, k)
                    if first:
                        h_rest(t, k)
                    if ahead:
                        if k == 0:
                            dve.wait_ge(s_x, 16 * (q + 1))
                        add_up(t + AHEAD, ka)
                    if not first:
                        h_rest(t, k)
                    if ahead:
                        centre(t + AHEAD, ka, first and k + AHEAD < U)

            nc.vector.memset(warm[:], 0.0).then_inc(s_warm, 1)
            for t in range(AHEAD):
                dve.wait_ge(s_x0[t], 16)
                add_up(t, t)
                centre(t, t, True)
            quad0(0, True, False)
            with dve.Fori(1, QUADS - 1) as q:
                quad0(q, False, False)
            quad0(QUADS - 1, False, True)
            dve.wait_ge(s_whi, 1)
            nc.vector.scalar_tensor_tensor(out=w_lo[:], in0=w_sb[:], scalar=D ** 0.5,
                                           in1=w_hi[:].bitcast(fp32),
                                           op0=ALU.mult, op1=ALU.subtract).then_inc(s_wlo, 1)

            def sums_rest(g):
                for i, (c, kb) in enumerate(GROUP_BANKS):
                    dve.wait_ge(s_ahi, g * SUMS + i + 1)
                    nc.vector.tensor_tensor(agg_lo[:, kb, chunk(c)], bank(g, kb, c)[:],
                                            agg_hi[:, kb, chunk(c)].bitcast(fp32),
                                            ALU.subtract).then_inc(s_alo, 1)

            def add_residual(g):
                dve.wait_ge(s_xt, 16 * (g + 1))
                for i, (c, o, a, b) in enumerate(pieces(g)):
                    cols = within(c, a, b)
                    dve.wait_ge(s_relu, g * SUMS + i + 1)
                    nc.vector.tensor_tensor(out_sb[:, o, cols], out_sb[:, o, cols],
                                            xt_sb[:, o, cols], ALU.add).then_inc(s_sum, 1)

            for g in range(1, GROUPS):
                for k in range(U):
                    adj_rest(g, 0, k)
                sums_rest(g - 1)
                for k in range(U):
                    adj_rest(g, 1, k)
                add_residual(g - 1)
                with dve.Fori(2, QUADS) as q:
                    for k in range(U):
                        adj_rest(g, q, k)
            sums_rest(LAST)
            add_residual(LAST)

        @block.scalar
        def _(act):
            def adj_rounded(g, q, k, fresh):
                n = g * TILES + q * U + k
                act.wait_ge(s_adj[k], 16 * (g * QUADS + q + (k > 0)))
                if not fresh:
                    act.wait_ge(s_pe, n - U + 1)
                nc.scalar.activation(adj_hi[:, k, :], adj_in[:, k, :], ACT.Copy).then_inc(s_hi, 1)

            def square_up(t, k, fresh):
                act.wait_ge(s_mean, t + 1)
                if not fresh:
                    act.wait_ge(s_rstd, t - U + 1)
                nc.scalar.activation(squares[:, k, :], x_sb[:, bass.ds(t, 1), :], ACT.Square,
                                     bias=neg_mean[:, k:k + 1], accum_out=square_sum[:, k:k + 1]
                                     ).then_inc(s_square, 1)

            def h_rounded(q, k, fresh):
                t = q * U + k
                act.wait_ge(s_rstd, t + 1)
                if not fresh:
                    act.wait_ge(s_pe, t - U + 1)
                    act.wait_ge(s_hst[k], 16 * q)
                act.wait_ge(s_centred, t + 1)
                nc.scalar.activation(h_ring[:, k, 0, :], centred[:, k, :],
                                     ACT.Copy, scale=rstd[:, k:k + 1]).then_inc(s_hhi, 1)

            def stage_h(q, k, fresh):
                if fresh:
                    act.wait_ge(s_hst[k], 16 * QUADS)
                nc.scalar.activation(h_ring[:, k, :, :], h_store[:, bass.ds(q * U + k, 1), :, :],
                                     ACT.Copy).then_inc(s_hring, 1)

            def quad0(q, first, last):
                for k in range(U):
                    if not (first and k == 0):
                        adj_rounded(0, q, k, first)
                        h_rounded(q, k, first)
                    if not (last and k + 1 == U):
                        square_up(q * U + k + 1, (k + 1) % U, first and k + 1 < U)

            square_up(0, 0, True)
            for c in range(CHUNKS):
                if c == 1:
                    h_rounded(0, 0, True)
                act.wait_ge(s_adj0[c], 16)
                done = nc.scalar.activation(adj_hi[:, 0, chunk(c)], adj_in[:, 0, chunk(c)], ACT.Copy)
                done.then_inc(s_hi if c == CHUNKS - 1 else s_hi0, 1)
            quad0(0, True, False)
            with act.Fori(1, QUADS - 1) as q:
                quad0(q, False, False)
            quad0(QUADS - 1, False, True)
            act.wait_ge(s_w, 16)
            nc.scalar.activation(w_hi[:], w_sb[:], ACT.Copy, scale=D ** 0.5).then_inc(s_whi, 1)

            def sums_rounded(g):
                if g >= 1:
                    act.wait_ge(s_prod, g * SUMS)
                if g < LAST:
                    act.wait_ge(s_pe, (g + 1) * TILES)
                for i, (c, kb) in enumerate(GROUP_BANKS):
                    if g == LAST:
                        act.wait_ge(s_chunk, c + 1)
                    nc.scalar.activation(agg_hi[:, kb, chunk(c)], bank(g, kb, c)[:], ACT.Copy
                                         ).then_inc(s_ahi, 1)

            def relu_out(g):
                if g >= 1:
                    act.wait_ge(s_out, 16 * g)
                for i, (c, o, a, b) in enumerate(pieces(g)):
                    act.wait_ge(s_prod, g * SUMS + i + 1)
                    nc.scalar.activation(out_sb[:, o, within(c, a, b)], product(g, c, o, a, b),
                                         ACT.Relu, bias=b_sb[:, o:o + 1]).then_inc(s_relu, 1)

            def quad(g, q, fresh):
                for k in range(U):
                    adj_rounded(g, q, k, False)
                    stage_h(q, k, fresh)

            act.wait_ge(s_b, 16)
            for g in range(1, GROUPS):
                quad(g, 0, g == 1)
                sums_rounded(g - 1)
                quad(g, 1, False)
                relu_out(g - 1)
                with act.Fori(2, QUADS) as q:
                    quad(g, q, False)
            sums_rounded(LAST)
            relu_out(LAST)

        @block.tensor
        def _(pe):
            PASSES = ((0, 0), (0, 1), (1, 0))
            adj_parts = (adj_hi, adj_lo)

            def sum_chunks(g, q, k, chunks, start, arrived):
                n = g * TILES + q * U + k
                first = g == 0 and start
                for kb in range(KB):
                    for hp, ap in PASSES:
                        if kb == 0 and not arrived:
                            if (hp, ap) == (0, 0):
                                if g == 0:
                                    pe.wait_ge(s_hhi, n + 1)
                                else:
                                    pe.wait_ge(s_hring, n - TILES + 1)
                                if not first:
                                    pe.wait_ge(s_hi, n + 1)
                            elif ap == 1:
                                pe.wait_ge(s_lo, n + 1)
                            elif g == 0:
                                pe.wait_ge(s_hlo, n + 1)
                        for c in chunks:
                            if first and kb == 0 and (hp, ap) == (0, 0):
                                if c < CHUNKS - 1:
                                    pe.wait_ge(s_hi0, c + 1)
                                else:
                                    pe.wait_ge(s_hi, 1)
                            last = nc.tensor.matmul(bank(g, kb, c)[:], h_ring[:, k, hp, kb * P:(kb + 1) * P],
                                                    adj_parts[ap][:, k, chunk(c)],
                                                    start=start and (hp, ap) == (0, 0),
                                                    stop=(hp == 1), skip_group_check=True)
                return last

            def quad(g, q, first):
                for k in range(U):
                    sum_chunks(g, q, k, range(CHUNKS), first and k == 0, False).then_inc(s_pe, 1)

            def last_quad():
                for c in range(CHUNKS):
                    for k in range(U):
                        last = sum_chunks(LAST, QUADS - 1, k, [c], False, c > 0)
                    last.then_inc(s_chunk, 1)

            def w_product(g):
                for c, o, a, b in pieces(g):
                    pe.wait_ge(s_alo, g * SUMS + (c + 1) * KB)
                    if a > 0:
                        pe.wait_ge(s_relu, g * SUMS)
                    for kb in range(KB):
                        for wp, ap in PASSES:
                            last = nc.tensor.matmul(product(g, c, o, a, b),
                                                    (w_hi, w_lo)[wp][:, kb, o * P:(o + 1) * P],
                                                    (agg_hi, agg_lo)[ap][:, kb, within(c, a, b)],
                                                    start=(kb == 0 and (wp, ap) == (0, 0)),
                                                    stop=(kb == KB - 1 and wp == 1))
                    last.then_inc(s_prod, 1)

            pe.wait_ge(s_warm, 1)
            for _ in range(WARM_UP):
                nc.tensor.matmul(bank(1, 0, 0)[:], warm[:, 0:P], warm[:], start=True, stop=True)
            quad(0, 0, True)
            with pe.Fori(1, QUADS) as q:
                quad(0, q, False)
            pe.wait_ge(s_wlo, 1)
            for g in range(1, GROUPS):
                if g >= 2:
                    pe.wait_ge(s_relu, (g - 1) * SUMS)
                quad(g, 0, True)
                w_product(g - 1)
                with pe.Fori(1, QUADS if g < LAST else QUADS - 1) as q:
                    quad(g, q, False)
            last_quad()
            w_product(LAST)


def kernel(x, adj, L0_gnn_W, L0_gnn_b):
    import numpy as np
    import concourse.bacc as bacc
    from concourse.bass_utils import run_bass_kernel_spmd

    x, adj, w, b = (np.asarray(a) for a in (x, adj, L0_gnn_W, L0_gnn_b))
    nodes, features = x.shape
    arrays = {
        "x_dram": np.ascontiguousarray(x),
        "x_t_dram": np.ascontiguousarray(x.T),
        "adj_t_dram": np.ascontiguousarray(adj.T),
        "w_t_dram": np.ascontiguousarray(w.T),
        "b_cols_dram": np.ascontiguousarray(b.reshape(features // P, P).T),
    }
    nc = bacc.Bacc("TRN2", target_bir_lowering=False, num_devices=1)
    args = [nc.dram_tensor(name, a.shape, mybir.dt.from_np(a.dtype), kind="ExternalInput").ap()
            for name, a in arrays.items()]
    out_t = nc.dram_tensor("out_t_dram", (features, nodes), mybir.dt.float32, kind="ExternalOutput").ap()
    bass_preln_gnn_residual(nc, *args, out_t)
    r = run_bass_kernel_spmd(nc, [arrays], core_ids=[0])
    return np.ascontiguousarray(r.results[0]["out_t_dram"].T)
```
